# Optimizing a Trainium2 kernel written in Bass

```python
import numpy as np
import jax
import jax.numpy as jnp

def _softmax(x, axis=-1):
    return jax.nn.softmax(x, axis=axis)

def _gelu(x):
    return jax.nn.gelu(x, approximate=True)

def _silu(x):
    return jax.nn.silu(x)

def _sigmoid(x):
    return jax.nn.sigmoid(x)

def _layernorm(x, axis=-1, eps=1e-05):
    m = jnp.mean(x, axis=axis, keepdims=True)
    v = jnp.var(x, axis=axis, keepdims=True)
    return (x - m) / jnp.sqrt(v + eps)

def _scatter_add(tgt, idx, src, axis=0):
    return tgt.at[idx].add(src)

def _segment_sum(src, seg, n):
    return jax.ops.segment_sum(src, seg, n)
kernel_name = 'mk_prb_d1_jaxref_r4_f3f054'

def setup_inputs(seed: int=0):
    np.random.seed(seed)
    _w = jnp.asarray

    def _L0_attn_setup():
        import jax, jax.numpy as jnp
        import numpy as np
        LN_EPS = 1e-05

        def _phi(x):
            return jax.nn.elu(x) + 1.0
        key = jax.random.key(seed)
        ks = jax.random.split(key, 5)
        B, N, D = (4, 2048, 256)
        s = 1.0 / np.sqrt(D)
        return {'H': jax.random.normal(ks[0], (B, N, D), dtype=jnp.float32), 'W_qkv': jax.random.normal(ks[1], (3 * D, D), dtype=jnp.float32) * s, 'b_qkv': jax.random.normal(ks[2], (3 * D,), dtype=jnp.float32) * 0.01, 'W_proj': jax.random.normal(ks[3], (D, D), dtype=jnp.float32) * s, 'b_proj': jax.random.normal(ks[4], (D,), dtype=jnp.float32) * 0.01, 'gamma': jnp.ones((D,), dtype=jnp.float32), 'beta': jnp.zeros((D,), dtype=jnp.float32)}
    _L0_attn_in = _L0_attn_setup()

    def _L0_ffn_setup():
        import jax, jax.numpy as jnp
        import numpy as np
        D_IN, D_HID = (256, 1024)

        def _ternary(key, shape):
            return jax.random.randint(key, shape, -1, 2).astype(jnp.float32)

        def _tlin(x, w, s):
            return jnp.einsum('bsi,oi->bso', x, w) * s
        key = jax.random.key(seed)
        ks = jax.random.split(key, 12)
        inv = lambda fan: 1.0 / np.sqrt(fan).astype(np.float32)
        return {'x': jax.random.normal(ks[0], (4, 512, D_IN), dtype=jnp.float32), 'w1_w': _ternary(ks[1], (D_HID, D_IN)), 'w1_s': jax.random.uniform(ks[2], (D_HID,), dtype=jnp.float32) * inv(D_IN), 'w2_w': _ternary(ks[3], (D_HID, D_IN)), 'w2_s': jax.random.uniform(ks[4], (D_HID,), dtype=jnp.float32) * inv(D_IN), 'h1_w': _ternary(ks[5], (D_HID, D_HID)), 'h1_s': jax.random.uniform(ks[6], (D_HID,), dtype=jnp.float32) * inv(D_HID), 'h2_w': _ternary(ks[7], (D_HID, D_HID)), 'h2_s': jax.random.uniform(ks[8], (D_HID,), dtype=jnp.float32) * inv(D_HID), 'w3_w': _ternary(ks[9], (D_IN, D_HID)), 'w3_s': jax.random.uniform(ks[10], (D_IN,), dtype=jnp.float32) * inv(D_HID)}
    _L0_ffn_in = _L0_ffn_setup()
    _d = {'L0_attn_H': _L0_attn_in['H'], 'L0_attn_W_qkv': _L0_attn_in['W_qkv'], 'L0_attn_b_qkv': _L0_attn_in['b_qkv'], 'L0_attn_W_proj': _L0_attn_in['W_proj'], 'L0_attn_b_proj': _L0_attn_in['b_proj'], 'L0_attn_gamma': _L0_attn_in['gamma'], 'L0_attn_beta': _L0_attn_in['beta'], 'L0_ffn_w1_w': _L0_ffn_in['w1_w'], 'L0_ffn_w1_s': _L0_ffn_in['w1_s'], 'L0_ffn_w2_w': _L0_ffn_in['w2_w'], 'L0_ffn_w2_s': _L0_ffn_in['w2_s'], 'L0_ffn_h1_w': _L0_ffn_in['h1_w'], 'L0_ffn_h1_s': _L0_ffn_in['h1_s'], 'L0_ffn_h2_w': _L0_ffn_in['h2_w'], 'L0_ffn_h2_s': _L0_ffn_in['h2_s'], 'L0_ffn_w3_w': _L0_ffn_in['w3_w'], 'L0_ffn_w3_s': _L0_ffn_in['w3_s']}
    _x0 = _d['L0_attn_H']
    _d['L0_attn_H'] = jax.random.normal(jax.random.fold_in(jax.random.key(seed), 1), (16, 512, 256), dtype=_x0.dtype)
    del _x0
    return _d

def reference(L0_attn_H, L0_attn_W_qkv, L0_attn_b_qkv, L0_attn_W_proj, L0_attn_b_proj, L0_attn_gamma, L0_attn_beta, L0_ffn_w1_w, L0_ffn_w1_s, L0_ffn_w2_w, L0_ffn_w2_s, L0_ffn_h1_w, L0_ffn_h1_s, L0_ffn_h2_w, L0_ffn_h2_s, L0_ffn_w3_w, L0_ffn_w3_s):

    def _L0_attn_ref(H, W_qkv, b_qkv, W_proj, b_proj, gamma, beta):
        import jax, jax.numpy as jnp
        import numpy as np
        LN_EPS = 1e-05

        def _phi(x):
            return jax.nn.elu(x) + 1.0
        B, N, D = H.shape
        num_heads = 16
        head_dim = D // num_heads
        residual = H
        qkv = jnp.einsum('bnd,ed->bne', H, W_qkv) + b_qkv
        qkv = qkv.reshape(B, N, 3, num_heads, head_dim).transpose(2, 0, 3, 1, 4)
        q, k, v = (qkv[0], qkv[1], qkv[2])
        q = _phi(q)
        k = _phi(k)
        kv = jnp.einsum('bhnd,bhnv->bhdv', k, v)
        k1 = k.sum(axis=2)
        qkv_out = jnp.einsum('bhnd,bhdv->bhnv', q, kv)
        qk1 = jnp.sum(q * k1[:, :, None, :], axis=-1, keepdims=True)
        out = qkv_out / jnp.clip(qk1, 1e-06, None)
        out = out.reshape(B, N, D)
        out = jnp.einsum('bnd,ed->bne', out, W_proj) + b_proj
        mu = out.mean(axis=-1, keepdims=True)
        var = out.var(axis=-1, keepdims=True)
        out = (out - mu) * jax.lax.rsqrt(var + LN_EPS) * gamma + beta
        return out + residual

    def _L0_ffn_ref(x, w1_w, w1_s, w2_w, w2_s, h1_w, h1_s, h2_w, h2_s, w3_w, w3_s):
        import jax, jax.numpy as jnp
        import numpy as np
        D_IN, D_HID = (256, 1024)

        def _ternary(key, shape):
            return jax.random.randint(key, shape, -1, 2).astype(jnp.float32)

        def _tlin(x, w, s):
            return jnp.einsum('bsi,oi->bso', x, w) * s
        h = jax.nn.silu(_tlin(x, w1_w, w1_s)) * _tlin(x, w2_w, w2_s)
        h = jax.nn.gelu(_tlin(h, h1_w, h1_s), approximate=False)
        h = jax.nn.gelu(_tlin(h, h2_w, h2_s), approximate=False)
        return _tlin(h, w3_w, w3_s)
    x = L0_attn_H
    xn = _layernorm(x, axis=-1)
    x = x + _L0_attn_ref(xn, L0_attn_W_qkv, L0_attn_b_qkv, L0_attn_W_proj, L0_attn_b_proj, L0_attn_gamma, L0_attn_beta) + _L0_ffn_ref(xn, L0_ffn_w1_w, L0_ffn_w1_s, L0_ffn_w2_w, L0_ffn_w2_s, L0_ffn_h1_w, L0_ffn_h1_s, L0_ffn_h2_w, L0_ffn_h2_s, L0_ffn_w3_w, L0_ffn_w3_s)
    return x

_drawn_inputs = setup_inputs


def setup_inputs(seed=0):
    import zlib

    import numpy as np

    out = dict(_drawn_inputs(seed))
    spreads = {'L0_attn_gamma': (1.0, 0.2), 'L0_attn_beta': (0.0, 0.1)}
    factors = {}
    for name, (base, spread) in spreads.items():
        noise = np.random.default_rng([zlib.crc32(name.encode()), seed]).standard_normal(out[name].shape)
        drawn = base * np.exp(spread * noise) if base else spread * noise
        out[name] = jnp.asarray(drawn.astype(out[name].dtype))
    for name, factor in factors.items():
        out[name] = (out[name] * factor).astype(out[name].dtype)
    return out
```

```python
import concourse.bass as bass
from concourse import mybir

F32 = mybir.dt.float32
F32R = mybir.dt.float32r
U32 = mybir.dt.uint32
I32 = mybir.dt.int32
ALU = mybir.AluOpType
ACT = mybir.ActivationFunctionType
AX_X = mybir.AxisListType.X

P = 128
B, N, D = 16, 512, 256
HID = 1024
HEADS = 16
TC = N // P
DC = D // P
HC = HID // P
EPS = 1e-5

W_GATE = 0
W_UP = W_GATE + DC * HID
W_HID1 = W_UP + DC * HID
W_HID2 = W_HID1 + HC * HID
W_OUT = W_HID2 + HC * HID
W_COLS = W_OUT + HC * D

V_GATE, V_UP, V_HID1, V_HID2, V_BQ = 0, HC, 2 * HC, 3 * HC, 4 * HC
V_COLS = 4 * HC + DC
R_OUT, R_GAMMA, R_BETA, R_BPROJ, R_BKV = 0, D, 2 * D, 3 * D, 4 * D
R_COLS = 6 * D

WARM_UP = 5
CHECKS = 4
CHECK_COLS = W_COLS // (B * CHECKS)

PAIRS = 3
G_HID1 = HC
G_HID2 = G_HID1 + HC // 2
G_OUT = G_HID2 + HC // 2
GROUPS = G_OUT + TC // 2
assert GROUPS % PAIRS == 0

(A_T0, A_T1,
 A_Q0, A_Q1,
 A_C0, A_C1, A_C2, A_C3,
 A_KV0, A_KV1,
 A_S0, A_S1, A_S2, A_S3,
 A_R0, A_R1,
 A_P0, A_P1) = range(18)
A_STEPS = A_P1 + 1

HH = HEADS // DC
VW = P + 2
KW = P + HH


class Count:

    def __init__(self, sem, per, credit=0, unit=1):
        self.sem, self.per, self.credit, self.unit = sem, per, credit, unit

    def at(self, t, n):
        return t * (self.per * self.unit) + (self.credit + n + 1) * self.unit


def block_kernel(nc, H, w_ffn, w_attn, vecs, rows, consts, out):
    x_dram = H.rearrange("b (c p) d -> b p c d", c=TC)
    out_dram = out.rearrange("b (c p) d -> b p c d", c=TC)

    top = [-(-nc.sbuf_base // 64) * 64]

    def sb(name, shape, dtype=F32, at=None):
        size = 4
        for n in shape[1:]:
            size *= n
        if at is None:
            at = top[0]
            top[0] += -(-size // 32) * 32
        return nc.alloc_sbuf_tensor_at(name, shape, dtype, offset=at)

    ffn_at = top[0]
    w = sb("w_ffn", [P, W_COLS], F32R)
    w_full = sb("w_ffn_full", [P, W_COLS], F32, at=ffn_at)
    wqkv = sb("wqkv_parts", [P, 2, DC, 3 * D], F32R)
    wproj = sb("wproj_parts", [P, 2, 2, D], F32R)
    rowv = sb("row_vectors", [P, R_COLS])
    vec = sb("vectors", [P, V_COLS])
    const = sb("constants", [P, 2 * P + HEADS // DC])
    ones = sb("ones", [P, 1])
    xnT = sb("xnT", [P, DC, 2, N], F32R)
    a_at = top[0]
    ha = sb("hidden_a", [P, HC, 2, N], F32R)
    b_at = top[0]
    hb = sb("hidden_b", [P, HC, 2, N], F32R)
    chunk = 2 * N * 4
    zkv = sb("zkv", [P, TC, 2 * DC, VW], at=b_at)
    e_tmp = sb("exp_tmp", [P, DC * N], at=b_at + 4 * TC * 2 * DC * VW)
    r_tmp = sb("relu_tmp", [P, DC * N], at=b_at + 4 * (TC * 2 * DC * VW + DC * N))
    kvb = sb("kv_by_head", [P, DC, KW], at=b_at + 4 * (TC * 2 * DC * VW + 2 * DC * N))
    ot = sb("attention_by_row", [P, 2, 2, N], F32R, at=b_at + 5 * chunk)
    q = sb("q", [P, DC, N], at=b_at + 7 * chunk)
    wqkv_raw = sb("wqkv_raw", [P, DC, 3 * D], at=a_at)
    wproj_raw = sb("wproj_raw", [P, 2, D], at=a_at + 4 * DC * 3 * D)
    x = sb("x", [P, TC, D])
    acc = sb("acc", [P, TC, D])
    xn = sb("xn", [P, TC, D])
    val = sb("value_ring", [P, 2, N])
    gate = sb("gate_ring", [P, 2, N])
    raw = sb("raw_weights", [P, CHECK_COLS], U32)
    low = sb("low_bits", [P, CHECK_COLS], U32)
    low_max = sb("low_bits_max", [P, 1])
    flag = sb("full_weights_needed", [1, 1], I32)
    bn = sb("bn_stats", [P, TC, 6])
    mv = sb("mean_var", [P, TC, 2])
    vare = sb("var_plus_eps", [P, TC])
    rstd = sb("rstd", [P, TC])
    power = sb("power", [P, TC])
    den = sb("denominators", [P, TC, HEADS])
    assert top[0] <= nc.sbuf_usable_end, top[0]

    ps = nc.alloc_psum_tensor("ps", [P, 8, N], F32)
    ident, heads_mask, own_head = const[:, 0:P], const[:, P:2 * P], const[:, 2 * P:]
    o_norm, o_swap = e_tmp, r_tmp

    def pair_bank(g, j):
        return ps[:, 2 * (g % PAIRS) + j, :]

    def att_bank(step):
        return ps[:, 2 * PAIRS + step % 2, :]

    def sem(name):
        return nc.alloc_semaphore(name)

    s_rows = sem("row_vectors_loaded")
    s_bias_kv = sem("kv_bias_loaded")
    s_vec = sem("vectors_loaded")
    s_const = sem("constants_loaded")
    s_qkv_raw = sem("qkv_weights_loaded")
    s_proj_raw = sem("proj_weights_loaded")
    w_pieces = [(W_GATE, W_HID1), (W_HID1, W_HID1 + 4 * HID), (W_HID1 + 4 * HID, W_HID2),
                (W_HID2, W_HID2 + 4 * HID), (W_HID2 + 4 * HID, W_OUT), (W_OUT, W_COLS)]
    s_w = [sem(f"ffn_weights_loaded_{i}") for i in range(len(w_pieces))]
    s_reload = sem("full_weights_loaded")
    s_hi_w = sem("wqkv_hi_made")
    s_wqkv = sem("wqkv_parts_made")
    s_wproj = sem("wproj_parts_made")
    s_zeros = sem("zeros_made")
    s_warm = sem("warm_up_done")
    s_ones = sem("ones_made")
    s_power = sem("power_made")
    s_low0 = sem("low_bits_cleared")
    s_low_step = sem("low_bits_reduced")
    s_flag_sum = sem("flag_summed")
    s_flag = sem("flag_made")

    x_loaded = Count(sem("x_loaded"), 1, unit=16)
    out_stored = Count(sem("out_stored"), 2, unit=16)
    acc_free = Count(sem("acc_free"), 1, 1)
    piece_loaded = Count(sem("raw_piece_loaded"), CHECKS, unit=16)
    piece_checked = Count(sem("raw_piece_checked"), CHECKS, 1)
    ffn_ready = Count(sem("ffn_group_ready"), GROUPS)
    half_ready = Count(sem("hidden_group_first_bank_ready"), HC)
    att_ready = Count(sem("attention_step_ready"), A_STEPS)
    silu_made = Count(sem("silu_made"), HC)
    gate_hi = Count(sem("gate_hi_made"), HC)
    gelu_made = Count(sem("gelu_made"), 2 * HC, 2 * HC)
    xnT_hi = Count(sem("xnT_hi_made"), DC)
    q_read = Count(sem("q_exp_relu_made"), DC)
    ot_hi = Count(sem("attention_by_row_hi"), 2)
    k_act = Count(sem("k_exp_relu_made"), TC)
    h_made = Count(sem("gated_value_made"), HC, HC)
    hid_hi = Count(sem("hidden_hi_made"), 2 * HC)
    split = Count(sem("hidden_split"), 3 * HC, 2)
    xnT_split = Count(sem("xnT_split"), DC)
    out_read = Count(sem("output_group_read"), TC // 2, TC // 2)
    out_made = Count(sem("output_half_made"), TC // 2)
    z_made = Count(sem("z_made"), TC)
    q_made = Count(sem("q_made"), DC)
    k_made = Count(sem("k_made"), TC)
    ones_put = Count(sem("ones_beside_v"), 1)
    kv_cut = Count(sem("kv_cut_to_heads"), 2 * DC)
    den_clipped = Count(sem("denominator_clipped"), TC)
    den_inverted = Count(sem("denominators_inverted"), 2)
    o_normed = Count(sem("attention_normalised"), TC)
    o_swapped = Count(sem("attention_swapped"), 1)
    ot_split = Count(sem("attention_by_row_split"), 2)
    ln1_stat = Count(sem("ln1_statistics"), 2 * TC)
    xn_made = Count(sem("xn_made"), TC)
    x_sum = Count(sem("x_plus_xn"), 2)
    o_made = Count(sem("attention_output_made"), 2, 2)
    ln1_var = Count(sem("ln1_var_plus_eps"), 1)
    ln2_var = Count(sem("ln2_var_plus_eps"), 1)
    ln2_stat = Count(sem("ln2_statistics"), 2 * TC)
    ln2_gain = Count(sem("ln2_gain_applied"), TC)
    acc_made = Count(sem("acc_made"), TC, TC)
    ln1_rstd = Count(sem("ln1_rstd_made"), 1)
    ln2_rstd = Count(sem("ln2_rstd_made"), 1)

    def bank_read(t, step):
        count, n = {A_T0: (xnT_split, 0), A_T1: (xnT_split, 1), A_Q0: (q_read, 0), A_Q1: (q_read, 1),
                    A_C0: (z_made, 0), A_C1: (z_made, 1), A_C2: (z_made, 2), A_C3: (z_made, 3),
                    A_KV0: (kv_cut, 1), A_KV1: (kv_cut, 3), A_S0: (o_normed, 0), A_S1: (o_normed, 1),
                    A_S2: (o_normed, 2), A_S3: (o_normed, 3), A_R0: (ot_split, 0), A_R1: (ot_split, 1),
                    A_P0: (o_made, 0), A_P1: (o_made, 1)}[step]
        return count.sem, count.at(t, n)

    def pair_read(t, g):
        g -= PAIRS
        if g < 0:
            g, t = g + GROUPS, t - 1
        if g < G_HID1:
            return h_made.sem, h_made.at(t, g)
        if g < G_OUT:
            return gelu_made.sem, gelu_made.at(t, 2 * (g - G_HID1) + 1)
        return out_read.sem, out_read.at(t, g - G_OUT)

    def halves(tmp, c):
        return tmp[:, c * D:(c + 1) * D].rearrange("p (h n) -> p h n", h=DC)

    def from_transposed(a0):
        return att_bank(A_R0 + a0).rearrange("p (sg v0 h) -> p v0 sg h", sg=16, v0=2)

    def by_row(part, a0):
        return ot[:, part].rearrange("p v0 (h sg a) -> p a v0 sg h", sg=16, a=2)[:, a0]

    def over_tiles(eng, first, prologue, body):
        prologue(first)
        with eng.Fori(first, first + B - 1) as t:
            body(t, True)
        body(first + B - 1, False)

    def second_pass_if_needed(eng, run):
        eng.wait_ge(s_flag, 1)
        need = eng.value_load(flag[0:1, 0:1])
        with eng.If(need != 0):
            run()

    block = nc.Block()
    with block:

        @block.sync
        def _(sp):
            sp.sem_inc(acc_free.sem, 1)

            def load_x(t, first):
                sp.wait_ge(acc_made.sem, acc_made.at(t - 1, TC - 1))
                sp.dma_start(x[:], of_tile(x_dram, t - first)).then_inc(x_loaded.sem, 16)

            def of_tile(dram, tile):
                return dram[tile] if isinstance(tile, int) else dram[bass.ds(tile, 1)][0]

            def body_of(first):
                def load_piece(t, j):
                    sp.wait_ge(piece_checked.sem, piece_checked.at(t, j - 1))
                    col = (t * CHECKS + j) * CHECK_COLS
                    src = w_ffn[:, col:col + CHECK_COLS] if isinstance(col, int) else w_ffn[:, bass.ds(col, CHECK_COLS)]
                    sp.dma_start(raw[:], src.bitcast(U32)).then_inc(piece_loaded.sem, 16)

                def body(t, more):
                    if first == 0:
                        load_piece(t, 0)
                    if more:
                        load_x(t + 1, first)
                    if first == 0:
                        for j in range(1, CHECKS):
                            load_piece(t, j)
                    for half in range(2):
                        two = slice(2 * half, 2 * half + 2)
                        sp.wait_ge(out_made.sem, out_made.at(t, half))
                        sp.dma_start(of_tile(out_dram, t - first)[:, two], acc[:, two]).then_inc(out_stored.sem, 16)
                    sp.wait_ge(out_stored.sem, out_stored.at(t, 1))
                    sp.sem_inc(acc_free.sem, 1)
                return body

            def prologue(t):
                load_x(t, 0)
                sp.dma_start(rowv[:, R_BKV:], rows[:, R_BKV:].to_broadcast([P, 2 * D])).then_inc(s_bias_kv, 16)
                sp.dma_start(vec[:], vecs).then_inc(s_vec, 16)
                sp.dma_start(rowv[:, :R_BKV], rows[:, :R_BKV].to_broadcast([P, R_BKV])).then_inc(s_rows, 16)

            over_tiles(sp, 0, prologue, body_of(0))

            def second():
                sp.dma_start(w_full[:], w_ffn).then_inc(s_reload, 16)
                over_tiles(sp, B, lambda t: load_x(t, B), body_of(B))
            second_pass_if_needed(sp, second)

        @block.gpsimd
        def _(pool):
            nc.gpsimd.memset(ones[:], 1.0).then_inc(s_ones, 1)
            nc.gpsimd.memset(power[:], -0.5).then_inc(s_power, 1)
            pool.wait_ge(x_loaded.sem, x_loaded.at(0, 0))

            def load_weights(i):
                lo, hi = w_pieces[i]
                pool.dma_start(w[:, lo:hi], w_ffn[:, lo:hi]).then_inc(s_w[i], 16)

            load_weights(0)
            pool.wait_ge(s_power, 1)

            def inverse_root(t, var, done):
                pool.wait_ge(var.sem, var.at(t, 0))
                nc.gpsimd.tensor_tensor(rstd[:], vare[:], power[:], ALU.pow).then_inc(done.sem, 1)

            def ln1(t):
                inverse_root(t, ln1_var, ln1_rstd)

            def body(t, more):
                inverse_root(t, ln2_var, ln2_rstd)
                if more:
                    ln1(t + 1)

            def prologue(t):
                ln1(t)
                for i in range(1, len(w_pieces)):
                    load_weights(i)

            over_tiles(pool, 0, prologue, body)
            second_pass_if_needed(pool, lambda: over_tiles(pool, B, ln1, body))

        @block.tensor
        def _(pe):
            pe.wait_ge(s_zeros, 1)
            for i in range(WARM_UP):
                nc.tensor.matmul(att_bank(A_P0), val[:, 0, 0:P], val[:, 1, :], start=True, stop=True).then_inc(s_warm, 1)

            mm = nc.tensor.matmul
            f = lambda ap: ap.bitcast(F32)

            def products(bank, weight, act, first, last, full):
                for part in range(2):
                    a, b = (weight, act(part)) if not full else (weight, f(act(part)))
                    r = mm(bank, a, b, start=first and part == 0, stop=last and part == 1)
                return r

            def three(bank, wh, wl, xh, xl, first, last):
                mm(bank, wl, xh, start=first, stop=False)
                mm(bank, wh, xl, start=False, stop=False)
                return mm(bank, wh, xh, start=False, stop=last)

            def transposes(t, c):
                if c == 0:
                    pe.wait_ge(xn_made.sem, xn_made.at(t, TC - 1))
                pe.wait_ge(*bank_read(t - 1, A_P0 + c))
                bank = att_bank(A_T0 + c)
                for k in range(TC):
                    r = nc.tensor.transpose(bank[:, k * P:(k + 1) * P], xn[:, k, c * P:(c + 1) * P], ident)
                r.then_inc(att_ready.sem, 1)

            def q_step(t, c):
                pe.wait_ge(*bank_read(t, A_T0 + c))
                bank = att_bank(A_Q0 + c)
                cols = slice(c * P, (c + 1) * P)
                for k in range(DC):
                    if c == 0:
                        pe.wait_ge(xnT_split.sem, xnT_split.at(t, k))
                    r = three(bank, wqkv[:, 0, k, cols], wqkv[:, 1, k, cols], xnT[:, k, 0, :], xnT[:, k, 1, :],
                              k == 0, k == DC - 1)
                r.then_inc(att_ready.sem, 1)

            def kv_step(t, c):
                pe.wait_ge(*bank_read(t, A_C0 + c - 2))
                bank = att_bank(A_C0 + c)
                toks = slice(c * P, (c + 1) * P)
                for k in range(DC):
                    r = three(bank, xnT[:, k, 0, toks], xnT[:, k, 1, toks], wqkv[:, 0, k, D:], wqkv[:, 1, k, D:],
                              k == 0, k == DC - 1)
                r.then_inc(att_ready.sem, 1)

            def kv_sums(t, h):
                if h == 0:
                    pe.wait_ge(k_made.sem, k_made.at(t, TC - 1))
                    pe.wait_ge(ones_put.sem, ones_put.at(t, 0))
                pe.wait_ge(*bank_read(t, A_C2 + h))
                for c in range(TC):
                    r = mm(att_bank(A_KV0 + h)[:, 0:P + 1], zkv[:, c, h, 0:P], zkv[:, c, DC + h, 0:P + 1],
                           start=c == 0, stop=c == TC - 1)
                r.then_inc(att_ready.sem, 1)

            def apply_kv(t, g):
                if g == 0:
                    pe.wait_ge(q_made.sem, q_made.at(t, DC - 1))
                    pe.wait_ge(kv_cut.sem, kv_cut.at(t, 2 * DC - 1))
                pe.wait_ge(*bank_read(t, A_S0 + g - 2))
                for h in range(DC):
                    r = mm(att_bank(A_S0 + g)[:, h * KW:(h + 1) * KW], q[:, h, g * P:(g + 1) * P], kvb[:, h, :],
                           start=True, stop=True)
                r.then_inc(att_ready.sem, 1)

            def to_rows(t, a0):
                if a0 == 0:
                    pe.wait_ge(o_swapped.sem, o_swapped.at(t, 0))
                pe.wait_ge(*bank_read(t, A_S2 + a0))
                swapped = o_swap[:].rearrange("p (s n a) -> p s n a", s=TC, a=2)
                for g in range(TC):
                    r = nc.tensor.transpose(att_bank(A_R0 + a0)[:, g * P:(g + 1) * P], swapped[:, g, :, a0], ident)
                r.then_inc(att_ready.sem, 1)

            def proj_step(t, half):
                if half == 0:
                    pe.wait_ge(s_wproj, 2)
                    pe.wait_ge(ot_split.sem, ot_split.at(t, 1))
                pe.wait_ge(*bank_read(t, A_R0 + half))
                for i in range(2):
                    rows_of = slice((2 * half + i) * P, (2 * half + i + 1) * P)
                    for v0 in range(2):
                        r = three(att_bank(A_P0 + half)[:, i * D:(i + 1) * D],
                                  ot[:, 0, v0, rows_of], ot[:, 1, v0, rows_of],
                                  wproj[:, 0, v0, :], wproj[:, 1, v0, :], v0 == 0, v0 == 1)
                r.then_inc(att_ready.sem, 1)

            def run(first, full):
                wt = w_full if full else w

                def gate_group(t, o):
                    if o == 0 and not full:
                        pe.wait_ge(s_w[0], 16)
                    pe.wait_ge(*pair_read(t, o))
                    for j, base in enumerate((W_GATE, W_UP)):
                        for k in range(DC):
                            r = products(pair_bank(o, j), wt[:, base + k * HID + o * P:base + k * HID + (o + 1) * P],
                                         lambda part: xnT[:, k, part, :], k == 0, k == DC - 1, full)
                    r.then_inc(ffn_ready.sem, 1)

                def hidden_group(t, stage, m):
                    base, src = ((W_HID1, ha), (W_HID2, hb))[stage]
                    g = G_HID1 + stage * (HC // 2) + m
                    pe.wait_ge(*pair_read(t, g))

                    def chunk_product(k, j):
                        o = 2 * m + j
                        return products(pair_bank(g, j), wt[:, base + k * HID + o * P:base + k * HID + (o + 1) * P],
                                        lambda part: src[:, k, part, :], k == 0, k == HC - 1, full)

                    if m == 0:
                        for k in range(HC):
                            if not full and k % 4 == 0:
                                pe.wait_ge(s_w[1 + 2 * stage + k // 4], 16)
                            pe.wait_ge(split.sem, split.at(t, stage * HC + k))
                            ends = [chunk_product(k, j) for j in range(2)]
                    else:
                        ends = []
                        for j in range(2):
                            for k in range(HC):
                                r = chunk_product(k, j)
                            ends.append(r)
                    ends[0].then_inc(half_ready.sem, 1)
                    ends[1].then_inc(ffn_ready.sem, 1)

                def out_group(t, m):
                    g = G_OUT + m
                    pe.wait_ge(*pair_read(t, g))
                    if m == 0 and not full:
                        pe.wait_ge(s_w[5], 16)
                    for k in range(HC):
                        if m == 0:
                            pe.wait_ge(split.sem, split.at(t, 2 * HC + k))
                        for j in range(2):
                            toks = slice((2 * m + j) * P, (2 * m + j + 1) * P)
                            wk = wt[:, W_OUT + k * D:W_OUT + (k + 1) * D]
                            for part in range(2):
                                a = ha[:, k, part, toks]
                                r = mm(pair_bank(g, j)[:, 0:D], f(a) if full else a, wk,
                                       start=k == 0 and part == 0, stop=k == HC - 1 and part == 1)
                    r.then_inc(ffn_ready.sem, 1)

                def prologue(t):
                    if full:
                        pe.wait_ge(s_reload, 16)
                    else:
                        pe.wait_ge(s_const, 16)
                        pe.wait_ge(s_ones, 1)
                    transposes(t, 0)
                    transposes(t, 1)
                    if not full:
                        pe.wait_ge(s_wqkv, 1)
                    q_step(t, 0)
                    q_step(t, 1)
                    for c in range(TC):
                        kv_step(t, c)

                def body(t, more):
                    gate_group(t, 0)
                    gate_group(t, 1)
                    kv_sums(t, 0)
                    kv_sums(t, 1)
                    gate_group(t, 2)
                    gate_group(t, 3)
                    apply_kv(t, 0)
                    apply_kv(t, 1)
                    gate_group(t, 4)
                    gate_group(t, 5)
                    gate_group(t, 6)
                    gate_group(t, 7)
                    apply_kv(t, 2)
                    apply_kv(t, 3)
                    hidden_group(t, 0, 0)
                    to_rows(t, 0)
                    to_rows(t, 1)
                    hidden_group(t, 0, 1)
                    proj_step(t, 0)
                    proj_step(t, 1)
                    hidden_group(t, 0, 2)
                    hidden_group(t, 0, 3)
                    hidden_group(t, 1, 0)
                    hidden_group(t, 1, 1)
                    if more:
                        transposes(t + 1, 0)
                        transposes(t + 1, 1)
                    hidden_group(t, 1, 2)
                    if not more and not full:
                        pe.wait_ge(s_low_step, 1)
                        pe.wait_ge(*bank_read(t, A_P0))
                        mm(att_bank(A_T0)[0:1, 0:1], low_max[:, 0:1], ones[:, 0:1],
                           start=True, stop=True).then_inc(s_flag_sum, 1)
                    hidden_group(t, 1, 3)
                    if more:
                        q_step(t + 1, 0)
                        q_step(t + 1, 1)
                    out_group(t, 0)
                    if more:
                        kv_step(t + 1, 0)
                        kv_step(t + 1, 1)
                    out_group(t, 1)
                    if more:
                        kv_step(t + 1, 2)
                        kv_step(t + 1, 3)

                over_tiles(pe, first, prologue, body)

            run(0, False)
            second_pass_if_needed(pe, lambda: run(B, True))

        @block.scalar
        def _(act):
            act.dma_start(const[:], consts).then_inc(s_const, 16)
            act.dma_start(wqkv_raw[:].rearrange("p k n -> p (k n)"), w_attn[:, 0:DC * 3 * D]).then_inc(s_qkv_raw, 16)
            act.dma_start(wproj_raw[:].rearrange("p k n -> p (k n)"), w_attn[:, DC * 3 * D:]).then_inc(s_proj_raw, 16)
            act.sem_inc(gelu_made.sem, gelu_made.credit)
            act.wait_ge(s_qkv_raw, 16)
            nc.scalar.activation(wqkv[:, 0], wqkv_raw[:], ACT.Copy).then_inc(s_hi_w, 1)
            act.wait_ge(s_vec, 16)

            def silu(t, o):
                act.wait_ge(ffn_ready.sem, ffn_ready.at(t, o))
                act.wait_ge(h_made.sem, h_made.at(t, o - 2))
                nc.scalar.activation(gate[:, o % 2, :], pair_bank(o, 0), ACT.Silu,
                                     scale=vec[:, V_GATE + o:V_GATE + o + 1]).then_inc(silu_made.sem, 1)

            def gated_hi(t, o):
                act.wait_ge(h_made.sem, h_made.at(t, o))
                nc.scalar.activation(ha[:, o, 0, :], val[:, o % 2, :], ACT.Copy).then_inc(gate_hi.sem, 1)

            def gelu_group(t, stage, m):
                g = G_HID1 + stage * (HC // 2) + m
                for j in range(2):
                    if j == 0:
                        act.wait_ge(half_ready.sem, half_ready.at(t, stage * (HC // 2) + m))
                    else:
                        act.wait_ge(ffn_ready.sem, ffn_ready.at(t, g))
                    o = 2 * m + j
                    n = (1 + stage) * HC + o
                    act.wait_ge(split.sem, split.at(t, n - 2))
                    col = (V_HID1, V_HID2)[stage] + o
                    nc.scalar.activation(val[:, n % 2, :], pair_bank(g, j), ACT.Gelu,
                                         scale=vec[:, col:col + 1]).then_inc(gelu_made.sem, 1)

            def transposed_hi(t, c):
                act.wait_ge(att_ready.sem, att_ready.at(t, A_T0 + c))
                nc.scalar.activation(xnT[:, c, 0, :], att_bank(A_T0 + c), ACT.Copy).then_inc(xnT_hi.sem, 1)

            def q_act(t, c):
                act.wait_ge(att_ready.sem, att_ready.at(t, A_Q0 + c))
                bias = vec[:, V_BQ + c:V_BQ + c + 1]
                tokens = att_bank(A_Q0 + c).rearrange("p (sg a b) -> p sg a b", sg=16, a=2)
                reorder = lambda tmp: tmp[:, c * N:(c + 1) * N].rearrange("p (sg b a) -> p sg a b", sg=16, a=2)
                nc.scalar.activation(reorder(e_tmp), tokens, ACT.Exp, bias=bias)
                nc.scalar.activation(reorder(r_tmp), tokens, ACT.Relu, bias=bias).then_inc(q_read.sem, 1)

            def k_act_step(t, c):
                act.wait_ge(z_made.sem, z_made.at(t, c))
                nc.scalar.activation(halves(e_tmp, c), zkv[:, c, 0:DC, 0:P], ACT.Exp)
                nc.scalar.activation(halves(r_tmp, c), zkv[:, c, 0:DC, 0:P], ACT.Relu).then_inc(k_act.sem, 1)

            def rows_hi(t, a0):
                act.wait_ge(att_ready.sem, att_ready.at(t, A_R0 + a0))
                nc.scalar.activation(by_row(0, a0), from_transposed(a0), ACT.Copy).then_inc(ot_hi.sem, 1)

            def prologue(t):
                transposed_hi(t, 0)
                transposed_hi(t, 1)
                q_act(t, 0)
                q_act(t, 1)
                for c in range(TC):
                    k_act_step(t, c)

            def body(t, more):
                for o in range(HC):
                    silu(t, o)
                    if o >= 1:
                        gated_hi(t, o - 1)
                gated_hi(t, HC - 1)
                gelu_group(t, 0, 0)
                rows_hi(t, 0)
                rows_hi(t, 1)
                for m in range(1, HC // 2):
                    gelu_group(t, 0, m)
                gelu_group(t, 1, 0)
                gelu_group(t, 1, 1)
                if more:
                    transposed_hi(t + 1, 0)
                    transposed_hi(t + 1, 1)
                gelu_group(t, 1, 2)
                gelu_group(t, 1, 3)
                if more:
                    q_act(t + 1, 0)
                    q_act(t + 1, 1)
                    for c in range(TC):
                        k_act_step(t + 1, c)

            over_tiles(act, 0, prologue, body)
            second_pass_if_needed(act, lambda: over_tiles(act, B, prologue, body))

        @block.vector
        def _(dve):
            v = nc.vector
            dve.sem_inc(o_made.sem, o_made.credit)
            dve.sem_inc(split.sem, split.credit)
            dve.sem_inc(h_made.sem, h_made.credit)
            dve.sem_inc(out_read.sem, out_read.credit)
            dve.sem_inc(acc_made.sem, acc_made.credit)
            dve.sem_inc(piece_checked.sem, piece_checked.credit)
            v.memset(val[:], 0.0).then_inc(s_zeros, 1)
            v.memset(low[:], 0).then_inc(s_low0, 1)

            def both(row):
                return rowv[:, row:row + D].unsqueeze(1).to_broadcast([P, 2, D])

            def aggregate(t, stats, done):
                dve.drain()
                for c in range(TC):
                    v.bn_aggr(mv[:, c, :], bn[:, c, :]).then_inc(stats.sem, 1)
                dve.wait_ge(stats.sem, stats.at(t, 2 * TC - 1))
                v.tensor_scalar(vare[:], mv[:, :, 1], EPS, None, ALU.add).then_inc(done.sem, 1)

            def ln1_stats(t):
                dve.wait_ge(x_loaded.sem, x_loaded.at(t, 0))
                for c in range(TC):
                    v.bn_stats(bn[:, c, :], x[:, c, :]).then_inc(ln1_stat.sem, 1)
                aggregate(t, ln1_stat, ln1_var)

            def ln1_apply(t):
                dve.wait_ge(ln1_rstd.sem, ln1_rstd.at(t, 0))
                for c in range(TC):
                    v.tensor_scalar(xn[:, c, :], x[:, c, :], mv[:, c, 0:1], rstd[:, c:c + 1],
                                    ALU.subtract, ALU.mult).then_inc(xn_made.sem, 1)

            def residual(t):
                dve.wait_ge(xn_made.sem, xn_made.at(t, TC - 1))
                v.tensor_tensor(x[:], x[:], xn[:], ALU.add).then_inc(x_sum.sem, 1)
                dve.wait_ge(x_sum.sem, x_sum.at(t, 0))
                beta = rowv[:, R_BETA:R_BETA + D].unsqueeze(1).to_broadcast([P, TC, D])
                v.tensor_tensor(x[:], x[:], beta, ALU.add).then_inc(x_sum.sem, 1)

            def transposed_lo(t, c):
                dve.wait_ge(xnT_hi.sem, xnT_hi.at(t, c))
                v.tensor_tensor(xnT[:, c, 1, :], att_bank(A_T0 + c), xnT[:, c, 0, :].bitcast(F32),
                                ALU.subtract).then_inc(xnT_split.sem, 1)

            def phi_q(t, c):
                dve.wait_ge(q_read.sem, q_read.at(t, c))
                cols = slice(c * N, (c + 1) * N)
                v.scalar_tensor_tensor(out=q[:, c, :], in0=e_tmp[:, cols], scalar=1.0, in1=r_tmp[:, cols],
                                       op0=ALU.min, op1=ALU.add).then_inc(q_made.sem, 1)

            def z_step(t, c):
                dve.wait_ge(att_ready.sem, att_ready.at(t, A_C0 + c))
                blocks = lambda ap: ap.rearrange("p (k n) -> p k n", k=2 * DC)
                v.tensor_tensor(zkv[:, c, :, 0:P], blocks(att_bank(A_C0 + c)), blocks(rowv[:, R_BKV:R_BKV + 2 * D]),
                                ALU.add).then_inc(z_made.sem, 1)

            def phi_k(t, c):
                dve.wait_ge(k_act.sem, k_act.at(t, c))
                v.scalar_tensor_tensor(out=zkv[:, c, 0:DC, 0:P], in0=halves(e_tmp, c), scalar=1.0, in1=halves(r_tmp, c),
                                       op0=ALU.min, op1=ALU.add).then_inc(k_made.sem, 1)

            def put_ones(t):
                v.memset(zkv[:, :, DC:, P:P + 1], 1.0).then_inc(ones_put.sem, 1)

            def cut_kv(t, h):
                dve.wait_ge(s_const, 16)
                dve.wait_ge(att_ready.sem, att_ready.at(t, A_KV0 + h))
                bank = att_bank(A_KV0 + h)
                v.tensor_tensor(kvb[:, h, 0:P], bank[:, 0:P], heads_mask, ALU.mult).then_inc(kv_cut.sem, 1)
                v.tensor_scalar(kvb[:, h, P:], own_head, bank[:, P:P + 1], None, ALU.mult).then_inc(kv_cut.sem, 1)

            def normalise(t, pair):
                groups = (2 * pair, 2 * pair + 1)
                parts = lambda g: att_bank(A_S0 + g)[:, 0:DC * KW].rearrange("p (h n) -> p h n", h=DC)
                for g in groups:
                    dve.wait_ge(att_ready.sem, att_ready.at(t, A_S0 + g))
                    v.tensor_scalar(den[:, g, :].rearrange("p (h n) -> p h n", h=DC), parts(g)[:, :, P:], 1e-6, None,
                                    ALU.max).then_inc(den_clipped.sem, 1)
                dve.wait_ge(den_clipped.sem, den_clipped.at(t, groups[1]))
                both_groups = den[:, groups[0]:groups[1] + 1, :]
                v.reciprocal(both_groups, both_groups).then_inc(den_inverted.sem, 1)
                dve.wait_ge(den_inverted.sem, den_inverted.at(t, pair))
                for g in groups:
                    inverse = den[:, g, :].rearrange("p (h n) -> p h n", h=DC).unsqueeze(3).to_broadcast([P, DC, HH, D // HEADS])
                    v.tensor_tensor(o_norm[:, g * D:(g + 1) * D].rearrange("p (v h n) -> p h n v", h=DC, n=HH),
                                    parts(g)[:, :, 0:P].rearrange("p h (n v) -> p h n v", n=HH), inverse,
                                    ALU.mult).then_inc(o_normed.sem, 1)

            def swap(t):
                dve.wait_ge(o_normed.sem, o_normed.at(t, TC - 1))
                v.transpose(o_swap[:], o_norm[:]).then_inc(o_swapped.sem, 1)

            def rows_lo(t, a0):
                dve.wait_ge(ot_hi.sem, ot_hi.at(t, a0))
                v.tensor_tensor(by_row(1, a0), from_transposed(a0), by_row(0, a0).bitcast(F32),
                                ALU.subtract).then_inc(ot_split.sem, 1)

            def gated(t, o):
                dve.wait_ge(split.sem, split.at(t, o - 2))
                dve.wait_ge(silu_made.sem, silu_made.at(t, o))
                v.scalar_tensor_tensor(out=val[:, o % 2, :], in0=pair_bank(o, 1), scalar=vec[:, V_UP + o:V_UP + o + 1],
                                       in1=gate[:, o % 2, :], op0=ALU.mult, op1=ALU.mult).then_inc(h_made.sem, 1)

            def gated_lo(t, o):
                dve.wait_ge(gate_hi.sem, gate_hi.at(t, o))
                v.tensor_tensor(ha[:, o, 1, :], val[:, o % 2, :], ha[:, o, 0, :].bitcast(F32),
                                ALU.subtract).then_inc(split.sem, 1)

            def split_group(t, stage, m):
                dst = (hb, ha)[stage]
                for j in range(2):
                    o = 2 * m + j
                    n = (1 + stage) * HC + o
                    dve.wait_ge(gelu_made.sem, gelu_made.at(t, stage * HC + o))
                    v.tensor_copy(dst[:, o, 0, :], val[:, n % 2, :]).then_inc(hid_hi.sem, 1)
                    dve.wait_ge(hid_hi.sem, hid_hi.at(t, stage * HC + o))
                    v.tensor_tensor(dst[:, o, 1, :], val[:, n % 2, :], dst[:, o, 0, :].bitcast(F32),
                                    ALU.subtract).then_inc(split.sem, 1)

            def ln2_stats(t):
                for half in range(2):
                    dve.wait_ge(att_ready.sem, att_ready.at(t, A_P0 + half))
                    v.tensor_tensor(xn[:, 2 * half:2 * half + 2, :],
                                    att_bank(A_P0 + half).rearrange("p (c d) -> p c d", c=2), both(R_BPROJ),
                                    ALU.add).then_inc(o_made.sem, 1)
                for c in range(TC):
                    if c % 2 == 0:
                        dve.wait_ge(o_made.sem, o_made.at(t, c // 2))
                    v.bn_stats(bn[:, c, :], xn[:, c, :]).then_inc(ln2_stat.sem, 1)
                aggregate(t, ln2_stat, ln2_var)

            def ln2_apply(t):
                dve.wait_ge(ln2_rstd.sem, ln2_rstd.at(t, 0))
                dve.wait_ge(acc_free.sem, acc_free.at(t - 1, 0))
                for c in range(TC):
                    v.scalar_tensor_tensor(out=xn[:, c, :], in0=xn[:, c, :], scalar=mv[:, c, 0:1],
                                           in1=rowv[:, R_GAMMA:R_GAMMA + D],
                                           op0=ALU.subtract, op1=ALU.mult).then_inc(ln2_gain.sem, 1)
                for c in range(TC):
                    if c == 0:
                        dve.wait_ge(ln2_gain.sem, ln2_gain.at(t, TC - 1))
                    v.scalar_tensor_tensor(out=acc[:, c, :], in0=xn[:, c, :], scalar=rstd[:, c:c + 1],
                                           in1=x[:, c, :], op0=ALU.mult, op1=ALU.add).then_inc(acc_made.sem, 1)

            def output(t, m):
                dve.wait_ge(ffn_ready.sem, ffn_ready.at(t, G_OUT + m))
                two = slice(2 * m, 2 * m + 2)
                first_bank = 2 * ((G_OUT + m) % PAIRS)
                v.tensor_tensor(xn[:, two, :], ps[:, first_bank:first_bank + 2, 0:D], both(R_OUT),
                                ALU.mult).then_inc(out_read.sem, 1)
                dve.wait_ge(out_read.sem, out_read.at(t, m))
                v.tensor_tensor(acc[:, two, :], acc[:, two, :], xn[:, two, :], ALU.add).then_inc(out_made.sem, 1)

            def check_piece(t, j):
                dve.wait_ge(piece_loaded.sem, piece_loaded.at(t, j))
                v.scalar_tensor_tensor(out=low[:], in0=raw[:], scalar=0xFFF, in1=low[:],
                                       op0=ALU.bitwise_and, op1=ALU.bitwise_or).then_inc(piece_checked.sem, 1)

            def split_qkv_weights():
                dve.wait_ge(s_hi_w, 1)
                v.tensor_tensor(wqkv[:, 1], wqkv_raw[:], wqkv[:, 0].bitcast(F32), ALU.subtract).then_inc(s_wqkv, 1)

            def split_proj_weights():
                dve.wait_ge(s_proj_raw, 16)
                v.tensor_copy(wproj[:, 0], wproj_raw[:]).then_inc(s_wproj, 1)
                dve.wait_ge(s_wproj, 1)
                v.tensor_tensor(wproj[:, 1], wproj_raw[:], wproj[:, 0].bitcast(F32), ALU.subtract).then_inc(s_wproj, 1)

            def run(first):
                checking = first == 0

                def prologue(t):
                    ln1_stats(t)
                    ln1_apply(t)
                    if checking:
                        split_qkv_weights()
                    transposed_lo(t, 0)
                    transposed_lo(t, 1)
                    phi_q(t, 0)
                    phi_q(t, 1)
                    put_ones(t)
                    if checking:
                        dve.wait_ge(s_bias_kv, 16)
                    for c in range(TC):
                        z_step(t, c)
                        if c >= 1:
                            phi_k(t, c - 1)
                    phi_k(t, TC - 1)
                    if checking:
                        dve.wait_ge(s_rows, 16)
                    residual(t)
                    if checking:
                        split_proj_weights()

                def body(t, more):
                    for o in range(HC):
                        gated(t, o)
                        if o >= 1:
                            gated_lo(t, o - 1)
                        if o == 1:
                            cut_kv(t, 0)
                            cut_kv(t, 1)
                        if o == 3:
                            normalise(t, 0)
                    gated_lo(t, HC - 1)
                    normalise(t, 1)
                    swap(t)
                    split_group(t, 0, 0)
                    rows_lo(t, 0)
                    rows_lo(t, 1)
                    if checking:
                        check_piece(t, 0)
                    split_group(t, 0, 1)
                    ln2_stats(t)
                    ln2_apply(t)
                    split_group(t, 0, 2)
                    if checking:
                        check_piece(t, 1)
                    if more:
                        ln1_stats(t + 1)
                    split_group(t, 0, 3)
                    if more:
                        ln1_apply(t + 1)
                        residual(t + 1)
                    split_group(t, 1, 0)
                    if checking:
                        check_piece(t, 2)
                        check_piece(t, 3)
                    split_group(t, 1, 1)
                    if more:
                        transposed_lo(t + 1, 0)
                        transposed_lo(t + 1, 1)
                    elif checking:
                        dve.wait_ge(piece_checked.sem, piece_checked.at(t, CHECKS - 1))
                        v.tensor_reduce(low_max[:], low[:], AX_X, ALU.max).then_inc(s_low_step, 1)
                    split_group(t, 1, 2)
                    if not more and checking:
                        dve.wait_ge(s_flag_sum, 1)
                        v.tensor_copy(flag[:], att_bank(A_T0)[0:1, 0:1]).then_inc(s_flag, 1)
                    split_group(t, 1, 3)
                    if more:
                        phi_q(t + 1, 0)
                        phi_q(t + 1, 1)
                        put_ones(t + 1)
                    output(t, 0)
                    if more:
                        z_step(t + 1, 0)
                        z_step(t + 1, 1)
                        phi_k(t + 1, 0)
                        phi_k(t + 1, 1)
                    output(t, 1)
                    if more:
                        z_step(t + 1, 2)
                        z_step(t + 1, 3)
                        phi_k(t + 1, 2)
                        phi_k(t + 1, 3)

                over_tiles(dve, first, prologue, body)

            dve.wait_ge(s_low0, 1)
            run(0)
            second_pass_if_needed(dve, lambda: run(B))


def kernel(**inputs):
    import numpy as _np
    import concourse.bacc as _bacc
    from concourse import mybir as _mybir
    from concourse.bass_utils import run_bass_kernel_spmd as _run

    def get(name):
        return _np.asarray(inputs["L0_" + name])

    def by_input(w):
        o, i = w.shape
        return w.T.reshape(i // P, P, o).transpose(1, 0, 2).reshape(P, -1)

    def by_partition(v):
        return v.reshape(-1, P).T

    b_qkv = get("attn_b_qkv")
    eye = _np.eye(P, dtype=_np.float32)
    head = _np.arange(P) // (D // HEADS)
    same_head = (head[:, None] == head[None, :]).astype(_np.float32)
    own_head = (head[:, None] == _np.arange(HEADS // DC)[None, :]).astype(_np.float32)
    w_proj = get("attn_W_proj").T.reshape(16, 8, 2, D).transpose(1, 0, 2, 3).reshape(P, -1)
    arrays = {
        "H": get("attn_H"),
        "w_ffn": _np.concatenate([by_input(get(n)) for n in
                                  ("ffn_w1_w", "ffn_w2_w", "ffn_h1_w", "ffn_h2_w", "ffn_w3_w")], axis=1),
        "w_attn": _np.concatenate([by_input(get("attn_W_qkv")), w_proj], axis=1),
        "vecs": _np.concatenate([by_partition(get(n)) for n in ("ffn_w1_s", "ffn_w2_s", "ffn_h1_s", "ffn_h2_s")]
                                + [by_partition(b_qkv[:D])], axis=1),
        "rows": _np.concatenate([get("ffn_w3_s"), get("attn_gamma"), get("attn_beta"), get("attn_b_proj"),
                                 b_qkv[D:]]).reshape(1, -1),
        "consts": _np.concatenate([eye, same_head, own_head], axis=1),
    }
    arrays = {f"in_{k}": _np.ascontiguousarray(v) for k, v in arrays.items()}
    nc = _bacc.Bacc("TRN2", target_bir_lowering=False, num_devices=1)
    args = [nc.dram_tensor(k, v.shape, _mybir.dt.from_np(v.dtype), kind="ExternalInput").ap() for k, v in arrays.items()]
    args.append(nc.dram_tensor("out_0_dram", (B, N, D), _mybir.dt.float32, kind="ExternalOutput").ap())
    block_kernel(nc, *args)
    r = _run(nc, [arrays], core_ids=[0])
    return r.results[0]["out_0_dram"]
```
